# Optimizing a Trainium2 kernel written in Bass

```python
import numpy as np
import jax
import jax.numpy as jnp

def _softmax(x, axis=-1):
    return jax.nn.softmax(x, axis=axis)

def _gelu(x):
    return jax.nn.gelu(x, approximate=True)

def _silu(x):
    return jax.nn.silu(x)

def _sigmoid(x):
    return jax.nn.sigmoid(x)

def _layernorm(x, axis=-1, eps=1e-05):
    m = jnp.mean(x, axis=axis, keepdims=True)
    v = jnp.var(x, axis=axis, keepdims=True)
    return (x - m) / jnp.sqrt(v + eps)

def _scatter_add(tgt, idx, src, axis=0):
    return tgt.at[idx].add(src)

def _segment_sum(src, seg, n):
    return jax.ops.segment_sum(src, seg, n)
kernel_name = 'mk_rec_standalone_d1_rec_r8_a6f00c'

def setup_inputs(seed: int=0):
    np.random.seed(seed)
    _w = jnp.asarray

    def _rec_inputs():
        import jax
        import jax.numpy as jnp
        _rk = jax.random.key(seed)
        r_sequence_ids = jax.random.randint(jax.random.fold_in(_rk, 1), (1024, 200), 35, 109962, jnp.int32)
        return r_sequence_ids
    r_sequence_ids = _rec_inputs()

    def _L0_rec_setup():
        import jax, jax.numpy as jnp
        import numpy as np
        N_ITEMS = 12500
        HIDDEN = 512
        BATCH = 64
        SEQ = 200
        key = jax.random.key(seed)
        k1, k2, k3 = jax.random.split(key, 3)
        sequence_ids = jax.random.randint(k1, (BATCH, SEQ), 0, 13750, dtype=jnp.int64 if jax.config.jax_enable_x64 else jnp.int32)
        emb_table = jax.random.normal(k2, (N_ITEMS, HIDDEN), dtype=jnp.float32) * 0.02
        proj_w = jax.random.normal(k3, (HIDDEN, N_ITEMS), dtype=jnp.float32) * 0.02
        proj_b = jnp.zeros((N_ITEMS,), dtype=jnp.float32)
        return {'sequence_ids': sequence_ids, 'emb_table': emb_table, 'proj_w': proj_w, 'proj_b': proj_b}
    _L0_rec_all = _L0_rec_setup()
    _L0_rec_in = {k: v for k, v in _L0_rec_all.items() if k in ('emb_table', 'proj_w', 'proj_b')}
    del _L0_rec_all
    return {'r_sequence_ids': r_sequence_ids, 'L0_rec_emb_table': _L0_rec_in['emb_table'], 'L0_rec_proj_w': _L0_rec_in['proj_w'], 'L0_rec_proj_b': _L0_rec_in['proj_b']}

def reference(r_sequence_ids, L0_rec_emb_table, L0_rec_proj_w, L0_rec_proj_b):
    import jax
    import jax.numpy as jnp

    def _L0_rec_ref(sequence_ids, emb_table, proj_w, proj_b):
        import jax, jax.numpy as jnp
        import numpy as np
        N_ITEMS = 12500
        HIDDEN = 512
        BATCH = 64
        SEQ = 200
        valid = sequence_ids < emb_table.shape[0]
        safe_ids = jnp.where(valid, sequence_ids, 0)
        seq_emb = emb_table[safe_ids]
        seq_emb = seq_emb * valid[..., None].astype(seq_emb.dtype)
        denom = jnp.maximum(valid.sum(axis=1, keepdims=True).astype(seq_emb.dtype), 1.0)
        user_repr = seq_emb.sum(axis=1) / denom
        logits = user_repr @ proj_w + proj_b
        return logits
    y = _L0_rec_ref(r_sequence_ids, L0_rec_emb_table, L0_rec_proj_w, L0_rec_proj_b)
    return y

_drawn_inputs = setup_inputs


def setup_inputs(seed=0):
    import zlib

    import numpy as np

    out = dict(_drawn_inputs(seed))
    spreads = {'L0_rec_proj_b': (0.0, 0.1)}
    factors = {'L0_rec_emb_table': 2.918, 'L0_rec_proj_w': 2.914}
    for name, (base, spread) in spreads.items():
        noise = np.random.default_rng([zlib.crc32(name.encode()), seed]).standard_normal(out[name].shape)
        drawn = base * np.exp(spread * noise) if base else spread * noise
        out[name] = jnp.asarray(drawn.astype(out[name].dtype))
    for name, factor in factors.items():
        out[name] = (out[name] * factor).astype(out[name].dtype)
    return out
```

```python
import concourse.bass as bass
from concourse import mybir
from contextlib import ExitStack


def mean_embedding_projection(nc, ids, table, proj, bias, out, FAST=40):
    F32, F32R = mybir.dt.float32, mybir.dt.float32r
    I32, U32 = mybir.dt.int32, mybir.dt.uint32
    ALU, ACT, AX = mybir.AluOpType, mybir.ActivationFunctionType, mybir.AxisListType

    P = 128
    USERS, SEQ = ids.shape
    ITEMS, HID = table.shape
    TILES = USERS // P
    K = HID // P
    TOP = 8
    CH = 5
    STEPS = 8
    assert FAST <= CH * STEPS and FAST % TOP == 0 and FAST % STEPS == 0
    CH = FAST // STEPS
    ROWS = 4
    BW = 500
    NB = ITEMS // BW
    GROUPS = [(0, 2), (2, 3), (5, 3)]
    LAST = len(GROUPS) - 1
    BLOCKS = NB * len(GROUPS)
    SEGS = NB // STEPS
    RAW, SPLIT, BIAS, STAGE, BANKS = 2, 4, 4, 2, 4
    FB = 4
    FB_ROUNDS = (SEQ - FAST) // TOP
    KEY_OPS = 4
    SORT_OPS = KEY_OPS + 2 * (FAST // TOP)
    assert NB * BW == ITEMS and NB == SEGS * STEPS + 1 and SEQ % TOP == 0
    assert all(GROUPS[g + 1][1] == SEGS for g in range(LAST))

    def product_base(g):
        return NB * sum(n for _, n in GROUPS[:g])

    w_view = proj.rearrange("(k p) n -> p k n", p=P)
    out_view = out.rearrange("(m p) n -> p m n", p=P)
    ids_view = ids.rearrange("(m p) s -> p m s", p=P)
    bias_view = bias.rearrange("(o n) -> o n", o=1)

    ctx = ExitStack()
    with ctx:
        def sb(name, shape, dt):
            return ctx.enter_context(nc.sbuf_tensor(name, shape, dt))

        def sem(name):
            return ctx.enter_context(nc.semaphore(name))

        ids_sb = sb("ids_sb", [P, TILES, SEQ], I32)
        shift = sb("shift", [P, SEQ], F32)
        key = sb("key", [P, SEQ], F32)
        top = sb("top", [P, FAST], F32)
        index = sb("index", [P, 2, FAST], U32)
        valid = sb("valid", [P, TILES, SEQ], F32)
        count = sb("count", [P, TILES], F32)
        count1 = sb("count1", [P, TILES], F32)
        inv_count = sb("inv_count", [P, TILES], F32)
        most = sb("most", [P, 1], F32)
        over = sb("over", [P, 1], F32)
        ones = sb("ones", [P, 1], F32)
        zero = sb("zero", [P, 1], F32)
        flag = sb("flag", [1, 1], I32)
        rows = sb("rows", [P, ROWS, CH + 1, HID], F32)
        total = sb("total", [P, HID], F32)
        mean = sb("mean", [P, HID], F32)
        ident = sb("ident", [P, P], F32)
        mean_hi = sb("mean_hi", [P, TILES, K, P], F32R)
        mean_lo = sb("mean_lo", [P, TILES, K, P], F32R)
        fb_key = sb("fb_key", [P, SEQ], F32)
        fb_top = sb("fb_top", [P, TOP], F32)
        fb_index = sb("fb_index", [P, TOP], U32)
        fb_rows = sb("fb_rows", [P, FB + 1, HID], F32)
        w_raw = sb("w_raw", [P, RAW, K, BW], F32)
        w_hi = sb("w_hi", [P, SPLIT, K, BW], F32R)
        w_lo = sb("w_lo", [P, SPLIT, K, BW], F32R)
        bias_sb = sb("bias_sb", [P, BIAS, BW], F32)
        stage = sb("stage", [P, STAGE, max(n for _, n in GROUPS), BW], F32)

        acc = ctx.enter_context(nc.psum_tensor("acc", [P, BANKS, 512], F32))
        turned = ctx.enter_context(nc.psum_tensor("turned", [P, K, P], F32))
        overs = ctx.enter_context(nc.psum_tensor("overs", [1, 512], F32))

        s_ids = sem("ids_loaded")
        s_const = sem("constants_set")
        s_ident = sem("identity_built")
        s_sort = sem("sort_steps")
        s_index = sem("index_ready")
        s_count = sem("count_steps")
        s_overs = sem("overs_summed")
        s_flag = sem("flag_ready")
        s_zeroed = sem("rows_zeroed")
        s_rows = [sem(f"rows_gathered{i}") for i in range(ROWS)]
        s_summed = sem("chunks_summed")
        s_total = sem("totals_ready")
        s_mean = sem("means_ready")
        s_turned = sem("means_turned")
        s_mean_hi = sem("mean_hi_ready")
        s_mean_lo = sem("mean_lo_ready")
        s_fb = sem("branch_steps")
        s_fb_go = sem("branch_index_ready")
        s_fb_rows = sem("branch_rows_gathered")
        s_pool_passed = sem("pool_passed")
        s_dve_passed = sem("dve_passed")
        s_raw = [sem(f"w_loaded{i}") for i in range(RAW)]
        s_bias = [sem(f"bias_loaded{i}") for i in range(BIAS)]
        s_w_hi = sem("w_hi_ready")
        s_w_lo = sem("w_lo_ready")
        s_product = sem("products_done")
        s_bank = sem("banks_freed")
        s_stored = [sem(f"stored{i}") for i in range(STAGE)]

        block = ctx.enter_context(nc.Block())

        @block.sync
        def _(sp):
            def one(g, b, lead_w, lead_bias):
                q = NB * g + b
                if q + lead_w < BLOCKS:
                    sp.wait_ge(s_w_lo, q + lead_w - RAW + 1)
                    sp.dma_start(w_raw[:, (q + lead_w) % RAW],
                                 w_view[:, :, bass.ts((b + lead_w) % NB, BW)]).then_inc(
                        s_raw[(q + lead_w) % RAW], 16)
                if q + lead_bias < BLOCKS:
                    sp.dma_start(bias_sb[:, (q + lead_bias) % BIAS],
                                 bias_view[:, bass.ts((b + lead_bias) % NB, BW)].to_broadcast([P, BW])).then_inc(
                        s_bias[(q + lead_bias) % BIAS], 16)
                first, n = GROUPS[g]
                sp.wait_ge(s_bank, BANKS + product_base(g) + n * (b + 1))
                sp.dma_start(out_view[:, first:first + n, bass.ts(b, BW)],
                             stage[:, q % STAGE, 0:n]).then_inc(s_stored[q % STAGE], 16)

            LEAD_W, LEAD_BIAS, UNROLL = 5, BIAS - 1, 4
            sp.dma_start(ids_sb[:], ids_view).then_inc(s_ids, 16)
            for q in range(LEAD_W):
                if q >= RAW:
                    sp.wait_ge(s_w_lo, q - RAW + 1)
                sp.dma_start(w_raw[:, q % RAW], w_view[:, :, bass.ts(q, BW)]).then_inc(s_raw[q % RAW], 16)
                if q < LEAD_BIAS:
                    sp.dma_start(bias_sb[:, q], bias_view[:, bass.ts(q, BW)].to_broadcast([P, BW])).then_inc(
                        s_bias[q], 16)
            for g, (first, n) in enumerate(GROUPS):
                looped = (NB - LEAD_W) // UNROLL
                with sp.Fori(0, looped) as i:
                    for j in range(UNROLL):
                        b = UNROLL * i + j
                        q = NB * g + j
                        sp.wait_ge(s_w_lo, UNROLL * i + (q + LEAD_W - RAW + 1))
                        sp.dma_start(w_raw[:, (q + LEAD_W) % RAW],
                                     w_view[:, :, bass.ds((b + LEAD_W) * BW, BW)]).then_inc(
                            s_raw[(q + LEAD_W) % RAW], 16)
                        sp.dma_start(bias_sb[:, (q + LEAD_BIAS) % BIAS],
                                     bias_view[:, bass.ds((b + LEAD_BIAS) * BW, BW)].to_broadcast([P, BW])).then_inc(
                            s_bias[(q + LEAD_BIAS) % BIAS], 16)
                        sp.wait_ge(s_bank, n * UNROLL * i + (BANKS + product_base(g) + n * (j + 1)))
                        sp.dma_start(out_view[:, first:first + n, bass.ds(b * BW, BW)],
                                     stage[:, q % STAGE, 0:n]).then_inc(s_stored[q % STAGE], 16)
                for b in range(UNROLL * looped, NB):
                    one(g, b, LEAD_W, LEAD_BIAS)
            for i in range(STAGE):
                sp.wait_ge(s_stored[i], 16 * len(range(i, BLOCKS, STAGE)))

        @block.gpsimd
        def _(pool):
            def alone():
                pool.sem_inc(s_pool_passed, 1)

            pool.memset(ident[:], 0.0).then_inc(s_ident, 1)
            pool.wait_ge(s_ident, 1)
            pool.affine_select(out=ident[:], in_=ident[:], compare_op=ALU.not_equal, fill=1.0, base=0,
                               pattern=[[-1, P]], channel_multiplier=1).then_inc(s_ident, 1)

            def gather(dst, column):
                return pool.indirect_dma_start(
                    out=dst, out_offset=None, in_=table,
                    in_offset=bass.IndirectOffsetOnAxis(ap=column, axis=0),
                    bounds_check=ITEMS - 1, oob_is_err=False)

            with pool.Fori(0, TILES // 2) as i:
                for parity in range(2):
                    t = 2 * i + parity
                    pool.wait_ge(s_index, t + 1)
                    for j in range(STEPS):
                        pool.wait_ge(s_zeroed, STEPS * t + (j + 1))
                        alone()
                        for c in range(CH):
                            gather(rows[:, j % ROWS, c, :], index[:, parity, CH * j + c:CH * j + c + 1]).then_inc(
                                s_rows[j % ROWS], 16)
                    pool.wait_ge(s_flag, 1)
                    more = pool.value_load(flag[0:1, 0:1], min_val=0, max_val=1)
                    with pool.If(more > 0):
                        with pool.Fori(0, FB_ROUNDS) as r:
                            for half in range(TOP // FB):
                                turn = (t * FB_ROUNDS + r) * (TOP // FB) + (half + 1)
                                pool.wait_ge(s_fb_go, turn)
                                alone()
                                for c in range(FB):
                                    gather(fb_rows[:, c, :], fb_index[:, FB * half + c:FB * half + c + 1]).then_inc(
                                        s_fb_rows, 16)

        @block.scalar
        def _(act):
            def clear(j):
                nc.scalar.activation(rows[:, j % ROWS, 0:CH, :].rearrange("p c d -> p (c d)"),
                                     zero[:, 0:1].to_broadcast([P, CH * HID]), ACT.Copy).then_inc(s_zeroed, 1)

            def w_high(q, i, per):
                act.wait_ge(s_raw[q % RAW], 16 * (per // RAW) * i + 16 * (q // RAW + 1))
                nc.scalar.activation(w_hi[:, q % SPLIT], w_raw[:, q % RAW], ACT.Copy).then_inc(s_w_hi, 1)

            def mean_high(t):
                act.wait_ge(s_turned, t + 1)
                nc.scalar.activation(mean_hi[:, bass.ds(t, 1)].rearrange("p o k u -> p (o k u)"),
                                     turned[:].rearrange("p k u -> p (k u)"), ACT.Copy).then_inc(s_mean_hi, 1)

            act.wait_ge(s_const, 1)
            for j in range(ROWS):
                clear(j)
            for q in range(RAW):
                w_high(q, 0, 0)
            first_tiles = GROUPS[0][1]
            for t in range(first_tiles):
                for j in range(STEPS):
                    act.wait_ge(s_summed, STEPS * t + j + 1)
                    clear(j)
                    if t == 0 and j < SPLIT - RAW:
                        w_high(RAW + j, 0, 0)
                mean_high(t)
            for g, (first, n) in enumerate(GROUPS):
                if g < LAST:
                    with act.Fori(0, SEGS) as i:
                        t = i + (first + n)
                        for j in range(STEPS):
                            act.wait_ge(s_summed, STEPS * t + (j + 1))
                            clear(j)
                            act.wait_ge(s_product, n * STEPS * i + (product_base(g) + n * (j + 1)))
                            w_high(NB * g + j + SPLIT, i, STEPS)
                        mean_high(t)
                    act.wait_ge(s_product, product_base(g + 1))
                    w_high(NB * g + NB - 1 + SPLIT, 0, 0)
                else:
                    left = NB - SPLIT
                    with act.Fori(0, left // SPLIT) as i:
                        for j in range(SPLIT):
                            act.wait_ge(s_product, n * SPLIT * i + (product_base(g) + n * (j + 1)))
                            w_high(NB * g + j + SPLIT, i, SPLIT)
                    for b in range(left // SPLIT * SPLIT, left):
                        act.wait_ge(s_product, product_base(g) + n * (b + 1))
                        w_high(NB * g + b + SPLIT, 0, 0)

        @block.vector
        def _(dve):
            def alone():
                dve.sem_inc(s_dve_passed, 1)

            def keys(dst, t, step, at):
                row = ids_sb[:, bass.ds(t, 1), :].rearrange("p o s -> p (o s)")
                dve.tensor_scalar(shift[:], row, 0.0, float(ITEMS), ALU.is_lt, ALU.mult).then_inc(step, 1)
                dve.wait_ge(step, at + 1)
                dve.tensor_tensor(dst, shift[:], row, ALU.add).then_inc(step, 1)
                dve.wait_ge(step, at + 2)
                dve.tensor_scalar(dst, dst, 0.0, -1.0, ALU.max, ALU.mult).then_inc(step, 1)
                dve.wait_ge(step, at + 3)
                dve.tensor_scalar(dst, dst, float(ITEMS), 0.0, ALU.add, ALU.max).then_inc(step, 1)
                dve.wait_ge(step, at + 4)
                alone()

            def sort(t, parity):
                at = SORT_OPS * t
                keys(key[:], t, s_sort, at)
                for r in range(FAST // TOP):
                    eight = top[:, TOP * r:TOP * (r + 1)]
                    dve.max(eight, key[:]).then_inc(s_sort, 1)
                    dve.wait_ge(s_sort, at + (KEY_OPS + 2 * r + 1))
                    alone()
                    dve.match_replace(key[:], eight, key[:], -1.0).then_inc(s_sort, 1)
                    dve.wait_ge(s_sort, at + (KEY_OPS + 2 * r + 2))
                    alone()
                dve.tensor_scalar(index[:, bass.ds(parity, 1), :].rearrange("p o f -> p (o f)"), top[:],
                                  -1.0, float(ITEMS), ALU.mult, ALU.add).then_inc(s_index, 1)

            def add_chunk(t, j):
                if j:
                    dve.wait_ge(s_summed, STEPS * t + j)
                dve.wait_ge(s_rows[j % ROWS], 16 * CH * (STEPS // ROWS) * t + 16 * CH * (j // ROWS + 1))
                n = CH + 1 if j else CH
                dst = rows[:, (j + 1) % ROWS, CH, :] if j < STEPS - 1 else total[:]
                dve.tensor_reduce(dst, rows[:, j % ROWS, 0:n, :].rearrange("p c d -> p d c"), AX.X,
                                  ALU.add).then_inc(s_summed, 1)

            def mean_of(t, more):
                dve.wait_ge(s_summed, STEPS * t + STEPS)
                alone()
                with dve.If(more > 0):
                    per_round = 2 + 2 * (TOP // FB)
                    per_tile = KEY_OPS + 2 * (FAST // TOP) + FB_ROUNDS * per_round
                    at = per_tile * t
                    keys(fb_key[:], t, s_fb, at)
                    at = at + KEY_OPS
                    for r in range(FAST // TOP):
                        dve.max(fb_top[:], fb_key[:]).then_inc(s_fb, 1)
                        dve.wait_ge(s_fb, at + (2 * r + 1))
                        alone()
                        dve.match_replace(fb_key[:], fb_top[:], fb_key[:], -1.0).then_inc(s_fb, 1)
                        dve.wait_ge(s_fb, at + (2 * r + 2))
                        alone()
                    at = at + 2 * (FAST // TOP)
                    with dve.Fori(0, FB_ROUNDS) as r:
                        step = at + per_round * r
                        dve.max(fb_top[:], fb_key[:]).then_inc(s_fb, 1)
                        dve.wait_ge(s_fb, step + 1)
                        alone()
                        dve.match_replace(fb_key[:], fb_top[:], fb_key[:], -1.0).then_inc(s_fb, 1)
                        dve.tensor_scalar(fb_index[:], fb_top[:], -1.0, float(ITEMS), ALU.mult, ALU.add)
                        for half in range(TOP // FB):
                            turn = (t * FB_ROUNDS + r) * (TOP // FB) + (half + 1)
                            dve.memset(fb_rows[:, 0:FB, :], 0.0).then_inc(s_fb_go, 1)
                            dve.wait_ge(s_fb_rows, 16 * FB * turn)
                            dve.tensor_reduce(fb_rows[:, FB, :], fb_rows[:, 0:FB, :].rearrange("p c d -> p d c"),
                                              AX.X, ALU.add).then_inc(s_fb, 1)
                            dve.wait_ge(s_fb, step + (2 + 2 * half + 1))
                            dve.tensor_tensor(total[:], total[:], fb_rows[:, FB, :], ALU.add).then_inc(s_fb, 1)
                            dve.wait_ge(s_fb, step + (2 + 2 * half + 2))
                            alone()
                dve.tensor_scalar(mean[:], total[:], inv_count[:, bass.ds(t, 1)], None, ALU.mult).then_inc(s_mean, 1)

            def mean_low(t):
                dve.wait_ge(s_mean_hi, t + 1)
                dve.tensor_tensor(mean_lo[:, bass.ds(t, 1)].rearrange("p o k u -> p (o k u)"),
                                  turned[:].rearrange("p k u -> p (k u)"),
                                  mean_hi[:, bass.ds(t, 1)].rearrange("p o k u -> p (o k u)").bitcast(F32),
                                  ALU.subtract).then_inc(s_mean_lo, 1)

            def w_low(q, i, per):
                dve.wait_ge(s_w_hi, per * i + (q + 1))
                dve.tensor_tensor(w_lo[:, q % SPLIT], w_raw[:, q % RAW], w_hi[:, q % SPLIT].bitcast(F32),
                                  ALU.subtract).then_inc(s_w_lo, 1)

            def move_out(g, j, i, per):
                n, q = GROUPS[g][1], NB * g + j
                if q >= STAGE:
                    dve.wait_ge(s_stored[q % STAGE], 16 * (per // STAGE) * i + 16 * (q // STAGE))
                elif per:
                    with dve.If(i > 0):
                        dve.wait_ge(s_stored[q % STAGE], 16 * (per // STAGE) * i)
                        alone()
                dve.wait_ge(s_bias[q % BIAS], 16 * (per // BIAS) * i + 16 * (q // BIAS + 1))
                for m in range(n):
                    r = product_base(g) + n * j + m
                    dve.wait_ge(s_product, n * per * i + (r + 1))
                    dve.tensor_tensor(stage[:, q % STAGE, m], acc[:, r % BANKS, 0:BW], bias_sb[:, q % BIAS],
                                      ALU.add).then_inc(s_bank, 1)

            dve.memset(zero[:], 0.0).then_inc(s_const, 1)
            dve.memset(ones[:], 1.0).then_inc(s_bank, BANKS)
            dve.wait_ge(s_ids, 16)
            sort(0, 0)
            sort(1, 1)
            dve.tensor_scalar(valid[:], ids_sb[:], float(ITEMS), None, ALU.is_lt).then_inc(s_count, 1)
            dve.wait_ge(s_count, 1)
            dve.tensor_reduce(count[:], valid[:], AX.X, ALU.add).then_inc(s_count, 1)
            dve.wait_ge(s_count, 2)
            dve.tensor_scalar(count1[:], count[:], 1.0, None, ALU.max).then_inc(s_count, 1)
            dve.tensor_reduce(most[:], count[:], AX.X, ALU.max).then_inc(s_count, 1)
            dve.wait_ge(s_count, 4)
            dve.reciprocal(inv_count[:], count1[:]).then_inc(s_count, 1)
            dve.tensor_scalar(over[:], most[:], float(FAST), None, ALU.is_gt).then_inc(s_count, 1)
            for q in range(RAW):
                w_low(q, 0, 0)
            dve.wait_ge(s_count, 6)
            dve.wait_ge(s_overs, 1)
            dve.tensor_scalar(flag[:], overs[0:1, 0:1], 1.0, None, ALU.min).then_inc(s_flag, 1)
            dve.wait_ge(s_flag, 1)
            more = dve.value_load(flag[0:1, 0:1], min_val=0, max_val=1)

            for t in range(GROUPS[0][1]):
                for j in range(STEPS):
                    add_chunk(t, j)
                    if t == 0 and j < SPLIT - RAW:
                        w_low(RAW + j, 0, 0)
                if t == 0:
                    sort(2, 0)
                mean_of(t, more)
                mean_low(t)
            for g, (first, n) in enumerate(GROUPS):
                if g < LAST:
                    with dve.Fori(0, SEGS) as i:
                        t = i + (first + n)
                        for j in range(STEPS):
                            add_chunk(t, j)
                            if j == 0:
                                if g < LAST - 1:
                                    sort(t + 1, (t + 1) % 2)
                                else:
                                    with dve.If(i < SEGS - 1):
                                        after = nc.s_assert_within(
                                            t + 1, 0, TILES - 1, skip_runtime_bounds_check_because="i < SEGS - 1")
                                        sort(after, after % 2)
                            if j == STEPS - 1:
                                mean_of(t, more)
                            move_out(g, j, i, STEPS)
                            w_low(NB * g + j + SPLIT, i, STEPS)
                        mean_low(t)
                    move_out(g, NB - 1, 0, 0)
                    w_low(NB * g + NB - 1 + SPLIT, 0, 0)
                else:
                    left = NB - SPLIT
                    with dve.Fori(0, left // SPLIT) as i:
                        for j in range(SPLIT):
                            move_out(g, j, i, SPLIT)
                            w_low(NB * g + j + SPLIT, i, SPLIT)
                    for b in range(left // SPLIT * SPLIT, NB):
                        move_out(g, b, 0, 0)
                        if b < left:
                            w_low(NB * g + b + SPLIT, 0, 0)

        @block.tensor
        def _(pe):
            def turn(t):
                pe.wait_ge(s_mean, t + 1)
                if not isinstance(t, int) or t:
                    pe.wait_ge(s_mean_lo, t)
                for k in range(K):
                    last = nc.tensor.transpose(turned[:, k], mean[:, k * P:(k + 1) * P], ident[:])
                last.then_inc(s_turned, 1)

            def products(g, j, i, per):
                (first, n), q = GROUPS[g], NB * g + j
                pe.wait_ge(s_w_lo, per * i + (q + 1))
                for m in range(n):
                    r = product_base(g) + n * j + m
                    pe.wait_ge(s_bank, n * per * i + (r + 1))
                    bank = acc[:, r % BANKS, 0:BW]
                    for k in range(K):
                        hi, lo = mean_hi[:, first + m, k], mean_lo[:, first + m, k]
                        nc.tensor.matmul(bank, hi, w_hi[:, q % SPLIT, k], start=k == 0, stop=False)
                        nc.tensor.matmul(bank, hi, w_lo[:, q % SPLIT, k], start=False, stop=False)
                        last = nc.tensor.matmul(bank, lo, w_hi[:, q % SPLIT, k], start=False, stop=k == K - 1)
                    last.then_inc(s_product, 1)

            pe.wait_ge(s_const, 1)
            pe.wait_ge(s_bank, BANKS)
            pe.wait_ge(s_count, 6)
            nc.tensor.matmul(overs[0:1, 0:1], over[:], ones[:], start=True, stop=True).then_inc(s_overs, 1)
            pe.wait_ge(s_ident, 2)
            for t in range(GROUPS[0][1]):
                turn(t)
            for g, (first, n) in enumerate(GROUPS):
                pe.wait_ge(s_mean_lo, first + n)
                if g < LAST:
                    with pe.Fori(0, SEGS) as i:
                        for j in range(STEPS):
                            products(g, j, i, STEPS)
                        turn(i + (first + n))
                    products(g, NB - 1, 0, 0)
                else:
                    with pe.Fori(0, NB // SPLIT) as i:
                        for j in range(SPLIT):
                            products(g, j, i, SPLIT)
                    for b in range(NB // SPLIT * SPLIT, NB):
                        products(g, b, 0, 0)


_INS = ["r_sequence_ids", "L0_rec_emb_table", "L0_rec_proj_w", "L0_rec_proj_b"]


def kernel(**inputs):
    import numpy as _np
    import concourse.bacc as _bacc
    from concourse import mybir as _mybir
    from concourse.bass_utils import run_bass_kernel_spmd as _run

    nc = _bacc.Bacc("TRN2", target_bir_lowering=False, num_devices=1)
    arrays, args = {}, []
    for name in _INS:
        a = _np.ascontiguousarray(inputs[name])
        arrays[f"in_{name}_dram"] = a
        args.append(nc.dram_tensor(f"in_{name}_dram", a.shape, _mybir.dt.from_np(a.dtype), kind="ExternalInput").ap())
    shape = (arrays["in_r_sequence_ids_dram"].shape[0], arrays["in_L0_rec_proj_w_dram"].shape[1])
    args.append(nc.dram_tensor("out_0_dram", shape, _mybir.dt.float32, kind="ExternalOutput").ap())
    mean_embedding_projection(nc, *args)
    r = _run(nc, [arrays], core_ids=[0])
    return r.results[0]["out_0_dram"]
```

```python
import concourse.bass as bass
from concourse import mybir
from contextlib import ExitStack


def mean_embedding_projection(nc, ids, table, proj, bias, out, FAST=40):
    F32, F32R = mybir.dt.float32, mybir.dt.float32r
    I32, U32 = mybir.dt.int32, mybir.dt.uint32
    ALU, ACT, AX = mybir.AluOpType, mybir.ActivationFunctionType, mybir.AxisListType

    P = 128
    USERS, SEQ = ids.shape
    ITEMS, HID = table.shape
    TILES = USERS // P
    K = HID // P
    TOP = 8
    BW = 500
    NB = ITEMS // BW
    SEG = 5
    STAY = NB // SEG
    SEGS = TILES - 1 + STAY
    BLOCKS = SEG * SEGS
    CH = FAST // SEG
    HALF = CH // 2
    CHUNKS = SEG * TILES
    AHEAD = SEG + 1
    RAW, SPLIT, BIAS, STAGE, ROWS, LISTS = 2, 4, 4, 2, 2, 2
    BANKS = 6
    LEAD_W, LEAD_BIAS = 5, 3
    FB = 4
    FB_ROUNDS = (SEQ - FAST) // TOP
    KEY_OPS = 4
    SORT_OPS = KEY_OPS + 2 * (FAST // TOP)
    assert NB * BW == ITEMS and NB == SEG * STAY and SEQ % TOP == 0 and FAST % TOP == 0
    assert CH * SEG == FAST and HALF * 2 == CH and TILES % LISTS == 0 and SEG % 2 == 1

    def tiles(s):
        first = max(0, s - STAY + 1)
        return first, min(TILES - 1, s) - first + 1

    def before(s):
        return SEG * sum(tiles(x)[1] for x in range(s))

    def after_block(q):
        return before(q // SEG) + tiles(q // SEG)[1] * (q % SEG + 1)

    w_view = proj.rearrange("(k p) n -> p k n", p=P)
    out_view = out.rearrange("(m p) n -> p m n", p=P)
    ids_view = ids.rearrange("(m p) s -> p m s", p=P)
    bias_view = bias.rearrange("(o n) -> o n", o=1)

    ctx = ExitStack()
    with ctx:
        def sb(name, shape, dt):
            return ctx.enter_context(nc.sbuf_tensor(name, shape, dt))

        def sem(name):
            return ctx.enter_context(nc.semaphore(name))

        ids_sb = sb("ids_sb", [P, TILES, SEQ], I32)
        shift = sb("shift", [P, SEQ], F32)
        key = sb("key", [P, SEQ], F32)
        top = sb("top", [P, FAST], F32)
        index = sb("index", [P, LISTS, FAST], U32)
        count = sb("count", [P, TILES], F32)
        count1 = sb("count1", [P, TILES], F32)
        inv_count = sb("inv_count", [P, TILES], F32)
        most = sb("most", [P, 1], F32)
        over = sb("over", [P, 1], F32)
        ones = sb("ones", [P, 1], F32)
        zero = sb("zero", [P, 1], F32)
        flag = sb("flag", [1, 1], I32)
        rows = sb("rows", [P, ROWS, CH + 1, HID], F32)
        total = sb("total", [P, HID], F32)
        mean = sb("mean", [P, HID], F32)
        ident = sb("ident", [P, P], F32)
        mean_hi = sb("mean_hi", [P, TILES, K * P], F32R)
        mean_lo = sb("mean_lo", [P, TILES, K * P], F32R)
        fb_key = sb("fb_key", [P, SEQ], F32)
        fb_top = sb("fb_top", [P, TOP], F32)
        fb_index = sb("fb_index", [P, TOP], U32)
        fb_rows = sb("fb_rows", [P, FB + 1, HID], F32)
        w_raw = sb("w_raw", [P, RAW, K, BW], F32)
        w_hi = sb("w_hi", [P, SPLIT, K, BW], F32R)
        w_lo = sb("w_lo", [P, SPLIT, K, BW], F32R)
        bias_sb = sb("bias_sb", [P, BIAS, BW], F32)
        stage = sb("stage", [P, STAGE, STAY, BW], F32)
        valid = stage[:, 0].rearrange("p m n -> p (m n)")[:, 0:TILES * SEQ].rearrange("p (t s) -> p t s", t=TILES)

        acc = ctx.enter_context(nc.psum_tensor("acc", [P, BANKS, 512], F32))
        turned = ctx.enter_context(nc.psum_tensor("turned", [P, K * P], F32))
        overs = ctx.enter_context(nc.psum_tensor("overs", [1, 512], F32))

        s_ids = sem("ids_loaded")
        s_const = sem("constants_set")
        s_ident = sem("identity_built")
        s_sort = sem("sort_steps")
        s_index = sem("index_ready")
        s_count = sem("count_steps")
        s_overs = sem("overs_summed")
        s_flag = sem("flag_ready")
        s_zeroed = sem("half_chunks_zeroed")
        s_rows = [sem(f"rows_gathered{i}") for i in range(ROWS)]
        s_summed = sem("chunks_summed")
        s_mean = sem("means_ready")
        s_turned = sem("means_turned")
        s_mean_hi = sem("mean_hi_ready")
        s_mean_lo = sem("mean_lo_ready")
        s_fb = sem("branch_steps")
        s_fb_go = sem("branch_index_ready")
        s_fb_rows = sem("branch_rows_gathered")
        s_pool_passed = sem("pool_passed")
        s_dve_passed = sem("dve_passed")
        s_raw = [sem(f"w_loaded{i}") for i in range(RAW)]
        s_bias = [sem(f"bias_loaded{i}") for i in range(BIAS)]
        s_w_hi = sem("w_hi_ready")
        s_w_lo = sem("w_lo_ready")
        s_product = sem("products_done")
        s_moved = sem("banks_freed")
        s_stored = [sem(f"stored{i}") for i in range(STAGE)]

        block = ctx.enter_context(nc.Block())

        @block.sync
        def _(sp):
            def load_w(q):
                if q >= RAW:
                    sp.wait_ge(s_w_lo, q - RAW + 1)
                sp.dma_start(w_raw[:, q % RAW], w_view[:, :, bass.ts(q % NB, BW)]).then_inc(s_raw[q % RAW], 16)

            def load_bias(q):
                if q >= BIAS:
                    sp.wait_ge(s_moved, BANKS + after_block(q - BIAS))
                sp.dma_start(bias_sb[:, q % BIAS],
                             bias_view[:, bass.ts(q % NB, BW)].to_broadcast([P, BW])).then_inc(s_bias[q % BIAS], 16)

            sp.dma_start(ids_sb[:], ids_view).then_inc(s_ids, 16)
            for q in range(LEAD_W):
                load_w(q)
                if q < LEAD_BIAS:
                    load_bias(q)
            for q in range(BLOCKS):
                if q + LEAD_W < BLOCKS:
                    load_w(q + LEAD_W)
                if q + LEAD_BIAS < BLOCKS:
                    load_bias(q + LEAD_BIAS)
                first, n = tiles(q // SEG)
                sp.wait_ge(s_moved, BANKS + after_block(q))
                sp.dma_start(out_view[:, first:first + n, bass.ts(q % NB, BW)],
                             stage[:, q % STAGE, 0:n]).then_inc(s_stored[q % STAGE], 16)
            for i in range(STAGE):
                sp.wait_ge(s_stored[i], 16 * len(range(i, BLOCKS, STAGE)))

        @block.gpsimd
        def _(pool):
            def alone():
                pool.sem_inc(s_pool_passed, 1)

            pool.memset(ident[:], 0.0).then_inc(s_ident, 1)
            pool.wait_ge(s_ident, 1)
            pool.affine_select(out=ident[:], in_=ident[:], compare_op=ALU.not_equal, fill=1.0, base=0,
                               pattern=[[-1, P]], channel_multiplier=1).then_inc(s_ident, 1)

            def gather(dst, column):
                return pool.indirect_dma_start(
                    out=dst, out_offset=None, in_=table,
                    in_offset=bass.IndirectOffsetOnAxis(ap=column, axis=0),
                    bounds_check=ITEMS - 1, oob_is_err=False)

            with pool.Fori(0, TILES // LISTS) as i:
                for parity in range(LISTS):
                    t = LISTS * i + parity
                    pool.wait_ge(s_index, t + 1)
                    for j in range(SEG):
                        buf = (SEG * parity + j) % ROWS
                        for c in range(CH):
                            if c % HALF == 0:
                                pool.wait_ge(s_zeroed, 2 * SEG * t + (2 * j + c // HALF + 1))
                                alone()
                            gather(rows[:, buf, c, :], index[:, parity, CH * j + c:CH * j + c + 1]).then_inc(
                                s_rows[buf], 16)
                    pool.wait_ge(s_flag, 1)
                    more = pool.value_load(flag[0:1, 0:1], min_val=0, max_val=1)
                    with pool.If(more > 0):
                        with pool.Fori(0, FB_ROUNDS) as r:
                            for half in range(TOP // FB):
                                turn = (t * FB_ROUNDS + r) * (TOP // FB) + (half + 1)
                                pool.wait_ge(s_fb_go, turn)
                                alone()
                                for c in range(FB):
                                    gather(fb_rows[:, c, :], fb_index[:, FB * half + c:FB * half + c + 1]).then_inc(
                                        s_fb_rows, 16)

        @block.scalar
        def _(act):
            def clear(c):
                if c >= ROWS:
                    act.wait_ge(s_summed, c - ROWS + 1)
                for h in range(2):
                    nc.scalar.activation(rows[:, c % ROWS, HALF * h:HALF * (h + 1), :].rearrange("p c d -> p (c d)"),
                                         zero[:, 0:1].to_broadcast([P, HALF * HID]), ACT.Copy).then_inc(s_zeroed, 1)

            def w_high(q):
                if q >= SPLIT:
                    act.wait_ge(s_product, after_block(q - SPLIT))
                act.wait_ge(s_raw[q % RAW], 16 * (q // RAW + 1))
                nc.scalar.activation(w_hi[:, q % SPLIT], w_raw[:, q % RAW], ACT.Copy).then_inc(s_w_hi, 1)

            def mean_high(t):
                act.wait_ge(s_turned, t + 1)
                nc.scalar.activation(mean_hi[:, t], turned[:], ACT.Copy).then_inc(s_mean_hi, 1)

            act.wait_ge(s_const, 1)
            for c in range(ROWS):
                clear(c)
            for q in range(RAW):
                w_high(q)
            for c in range(AHEAD):
                clear(c + ROWS)
                if RAW <= c + 1 < SPLIT:
                    w_high(c + 1)
                if c == SEG - 1:
                    mean_high(0)
            for q in range(BLOCKS):
                c = q + AHEAD
                if c + ROWS < CHUNKS:
                    clear(c + ROWS)
                if q + SPLIT < BLOCKS:
                    w_high(q + SPLIT)
                if c < CHUNKS and c % SEG == SEG - 1:
                    mean_high(c // SEG)

        @block.vector
        def _(dve):
            def alone():
                dve.sem_inc(s_dve_passed, 1)

            def keys(dst, t, step, at):
                dve.tensor_scalar(shift[:], ids_sb[:, t], 0.0, float(ITEMS), ALU.is_lt, ALU.mult).then_inc(step, 1)
                dve.wait_ge(step, at + 1)
                dve.tensor_tensor(dst, shift[:], ids_sb[:, t], ALU.add).then_inc(step, 1)
                dve.wait_ge(step, at + 2)
                dve.tensor_scalar(dst, dst, 0.0, -1.0, ALU.max, ALU.mult).then_inc(step, 1)
                dve.wait_ge(step, at + 3)
                dve.tensor_scalar(dst, dst, float(ITEMS), 0.0, ALU.add, ALU.max).then_inc(step, 1)
                dve.wait_ge(step, at + 4)

            def sort(t):
                at = SORT_OPS * t
                keys(key[:], t, s_sort, at)
                for r in range(FAST // TOP):
                    eight = top[:, TOP * r:TOP * (r + 1)]
                    dve.max(eight, key[:]).then_inc(s_sort, 1)
                    dve.wait_ge(s_sort, at + KEY_OPS + 2 * r + 1)
                    dve.match_replace(key[:], eight, key[:], -1.0).then_inc(s_sort, 1)
                    dve.wait_ge(s_sort, at + KEY_OPS + 2 * r + 2)
                dve.tensor_scalar(index[:, t % LISTS], top[:], -1.0, float(ITEMS), ALU.mult, ALU.add).then_inc(
                    s_index, 1)

            def add_chunk(c):
                j = c % SEG
                if j:
                    dve.wait_ge(s_summed, c)
                dve.wait_ge(s_rows[c % ROWS], 16 * CH * (c // ROWS + 1))
                n = CH + 1 if j else CH
                dst = rows[:, (c + 1) % ROWS, CH, :] if j < SEG - 1 else total[:]
                dve.tensor_reduce(dst, rows[:, c % ROWS, 0:n, :].rearrange("p c d -> p d c"), AX.X,
                                  ALU.add).then_inc(s_summed, 1)

            def mean_of(t, more):
                dve.wait_ge(s_summed, SEG * (t + 1))
                with dve.If(more > 0):
                    per_round = 2 + 2 * (TOP // FB)
                    at = (KEY_OPS + 2 * (FAST // TOP) + FB_ROUNDS * per_round) * t
                    keys(fb_key[:], t, s_fb, at)
                    at += KEY_OPS
                    for r in range(FAST // TOP):
                        dve.max(fb_top[:], fb_key[:]).then_inc(s_fb, 1)
                        dve.wait_ge(s_fb, at + 2 * r + 1)
                        dve.match_replace(fb_key[:], fb_top[:], fb_key[:], -1.0).then_inc(s_fb, 1)
                        dve.wait_ge(s_fb, at + 2 * r + 2)
                    at += 2 * (FAST // TOP)
                    with dve.Fori(0, FB_ROUNDS) as r:
                        step = per_round * r + at
                        dve.max(fb_top[:], fb_key[:]).then_inc(s_fb, 1)
                        dve.wait_ge(s_fb, step + 1)
                        alone()
                        dve.match_replace(fb_key[:], fb_top[:], fb_key[:], -1.0).then_inc(s_fb, 1)
                        dve.tensor_scalar(fb_index[:], fb_top[:], -1.0, float(ITEMS), ALU.mult, ALU.add)
                        for half in range(TOP // FB):
                            turn = (TOP // FB) * r + (t * FB_ROUNDS * (TOP // FB) + half + 1)
                            dve.memset(fb_rows[:, 0:FB, :], 0.0).then_inc(s_fb_go, 1)
                            dve.wait_ge(s_fb_rows, 16 * FB * turn)
                            dve.tensor_reduce(fb_rows[:, FB, :], fb_rows[:, 0:FB, :].rearrange("p c d -> p d c"),
                                              AX.X, ALU.add).then_inc(s_fb, 1)
                            dve.wait_ge(s_fb, step + (2 + 2 * half + 1))
                            dve.tensor_tensor(total[:], total[:], fb_rows[:, FB, :], ALU.add).then_inc(s_fb, 1)
                            dve.wait_ge(s_fb, step + (2 + 2 * half + 2))
                            alone()
                dve.tensor_scalar(mean[:], total[:], inv_count[:, t:t + 1], None, ALU.mult).then_inc(s_mean, 1)

            def mean_low(t):
                dve.wait_ge(s_mean_hi, t + 1)
                dve.tensor_tensor(mean_lo[:, t], turned[:], mean_hi[:, t].bitcast(F32), ALU.subtract).then_inc(
                    s_mean_lo, 1)

            def w_low(q):
                dve.wait_ge(s_w_hi, q + 1)
                dve.tensor_tensor(w_lo[:, q % SPLIT], w_raw[:, q % RAW], w_hi[:, q % SPLIT].bitcast(F32),
                                  ALU.subtract).then_inc(s_w_lo, 1)

            def move_out(q):
                first, n = tiles(q // SEG)
                dve.wait_ge(s_bias[q % BIAS], 16 * (q // BIAS + 1))
                if q >= STAGE:
                    dve.wait_ge(s_stored[q % STAGE], 16 * (q // STAGE))
                for r in range(after_block(q) - n, after_block(q)):
                    m = r - (after_block(q) - n)
                    dve.wait_ge(s_product, r + 1)
                    dve.tensor_tensor(stage[:, q % STAGE, m], acc[:, r % BANKS, 0:BW],
                                      bias_sb[:, q % BIAS], ALU.add).then_inc(s_moved, 1)

            dve.memset(zero[:], 0.0).then_inc(s_const, 1)
            dve.memset(ones[:], 1.0).then_inc(s_moved, BANKS)
            dve.wait_ge(s_ids, 16)
            sort(0)
            sort(1)
            dve.tensor_scalar(valid, ids_sb[:], float(ITEMS), None, ALU.is_lt).then_inc(s_count, 1)
            dve.wait_ge(s_count, 1)
            dve.tensor_reduce(count[:], valid, AX.X, ALU.add).then_inc(s_count, 1)
            dve.wait_ge(s_count, 2)
            dve.tensor_scalar(count1[:], count[:], 1.0, None, ALU.max).then_inc(s_count, 1)
            dve.tensor_reduce(most[:], count[:], AX.X, ALU.max).then_inc(s_count, 1)
            dve.wait_ge(s_count, 4)
            dve.reciprocal(inv_count[:], count1[:]).then_inc(s_count, 1)
            dve.tensor_scalar(over[:], most[:], float(FAST), None, ALU.is_gt).then_inc(s_count, 1)
            add_chunk(0)
            w_low(0)
            dve.wait_ge(s_count, 6)
            dve.wait_ge(s_overs, 1)
            dve.tensor_scalar(flag[:], overs[0:1, 0:1], 1.0, None, ALU.min).then_inc(s_flag, 1)
            dve.wait_ge(s_flag, 1)
            more = dve.value_load(flag[0:1, 0:1], min_val=0, max_val=1)
            for c in range(1, AHEAD):
                add_chunk(c)
                if c < SPLIT:
                    w_low(c)
                if c == SEG - 1:
                    mean_of(0, more)
                    mean_low(0)
            sort(2)
            for q in range(BLOCKS):
                c = q + AHEAD
                if c < CHUNKS:
                    add_chunk(c)
                    if c % SEG == 0 and c // SEG + 1 < TILES:
                        sort(c // SEG + 1)
                    if c % SEG == SEG - 1:
                        mean_of(c // SEG, more)
                move_out(q)
                if q + SPLIT < BLOCKS:
                    w_low(q + SPLIT)
                if c < CHUNKS and c % SEG == SEG - 1:
                    mean_low(c // SEG)

        @block.tensor
        def _(pe):
            def turn(t):
                pe.wait_ge(s_mean, t + 1)
                if t:
                    pe.wait_ge(s_mean_lo, t)
                for k in range(K):
                    last = nc.tensor.transpose(turned[:, k * P:(k + 1) * P], mean[:, k * P:(k + 1) * P], ident[:])
                last.then_inc(s_turned, 1)

            def products(s, j):
                first, n = tiles(s)
                pe.wait_ge(s_w_lo, j + (SEG * s + 1))
                buf = (j + SEG * s) % SPLIT
                for m in range(n):
                    r = j * n + (before(s) + m)
                    pe.wait_ge(s_moved, r + 1)
                    bank = acc[:, bass.ds(r % BANKS, 1), 0:BW].rearrange("p o n -> p (o n)")
                    for k in range(K):
                        hi, lo = (x[:, first + m, k * P:(k + 1) * P] for x in (mean_hi, mean_lo))
                        high, low = (x[:, bass.ds(buf, 1), k].rearrange("p o n -> p (o n)") for x in (w_hi, w_lo))
                        nc.tensor.matmul(bank, hi, high, start=k == 0, stop=False)
                        nc.tensor.matmul(bank, hi, low, start=False, stop=False)
                        last = nc.tensor.matmul(bank, lo, high, start=False, stop=k == K - 1)
                    last.then_inc(s_product, 1)

            pe.wait_ge(s_count, 6)
            pe.wait_ge(s_moved, BANKS)
            nc.tensor.matmul(overs[0:1, 0:1], over[:], ones[:], start=True, stop=True).then_inc(s_overs, 1)
            pe.wait_ge(s_ident, 2)
            turn(0)
            for s in range(SEGS):
                pe.wait_ge(s_mean_lo, min(s + 1, TILES))
                if s + 1 < TILES:
                    with pe.Fori(0, SEG - 1) as j:
                        products(s, j)
                    turn(s + 1)
                    products(s, SEG - 1)
                else:
                    with pe.Fori(0, SEG) as j:
                        products(s, j)


_INS = ["r_sequence_ids", "L0_rec_emb_table", "L0_rec_proj_w", "L0_rec_proj_b"]


def kernel(**inputs):
    import numpy as _np
    import concourse.bacc as _bacc
    from concourse import mybir as _mybir
    from concourse.bass_utils import run_bass_kernel_spmd as _run

    nc = _bacc.Bacc("TRN2", target_bir_lowering=False, num_devices=1)
    arrays, args = {}, []
    for name in _INS:
        a = _np.ascontiguousarray(inputs[name])
        arrays[f"in_{name}_dram"] = a
        args.append(nc.dram_tensor(f"in_{name}_dram", a.shape, _mybir.dt.from_np(a.dtype), kind="ExternalInput").ap())
    shape = (arrays["in_r_sequence_ids_dram"].shape[0], arrays["in_L0_rec_proj_w_dram"].shape[1])
    args.append(nc.dram_tensor("out_0_dram", shape, _mybir.dt.float32, kind="ExternalOutput").ap())
    mean_embedding_projection(nc, *args)
    r = _run(nc, [arrays], core_ids=[0])
    return r.results[0]["out_0_dram"]
```

```python
import concourse.bass as bass
from concourse import mybir
from contextlib import ExitStack


def mean_embedding_projection(nc, ids, table, proj, bias, out, FAST=36,
                              JOIN=(0, 5, 10, 15, 20, 25, 29, 33)):
    F32, F32R, BF16 = mybir.dt.float32, mybir.dt.float32r, mybir.dt.bfloat16
    I32, U32 = mybir.dt.int32, mybir.dt.uint32
    ALU, ACT, AX = mybir.AluOpType, mybir.ActivationFunctionType, mybir.AxisListType

    P = 128
    USERS, SEQ = ids.shape
    ITEMS, HID = table.shape
    TILES = USERS // P
    K = HID // P
    TOP = 8
    BW = 500
    NB = ITEMS // BW
    CH = 4
    BACK = 2
    TURNS = TOP // BACK
    LISTED = -(-FAST // TOP) * TOP
    PARTS = FAST // CH
    CHUNKS = PARTS * TILES
    SORT_AT = (1, 2, 3, 4, 5)
    BLOCKS = JOIN[-1] + NB
    RAW, SPLIT, BIAS, STAGE, ROWS, LISTS = 2, 4, 3, 2, 4, 2
    POOL_TILES = 4
    BANKS = 6
    LEAD_W = SPLIT - 1 + RAW
    LEAD_BIAS = 2
    PART_AT = (0, 32, 64)
    BIAS_ROWS = PART_AT[-1] + NB
    LEAD_LOW = SPLIT - 1
    HIGH_AFTER, LOW_AFTER, BIAS_AFTER = (5, 7), (4, 6), (2, 3)
    MORE = -(-(SEQ - FAST) // TOP)
    AGAIN = LISTED - FAST
    KEY_OPS = 4
    SORT_OPS = KEY_OPS + 2 * (LISTED // TOP)
    assert NB <= PART_AT[1] and BIAS_ROWS <= P
    assert NB * BW == ITEMS and PARTS * CH == FAST and TOP % CH == 0 and CH == 4 and PARTS >= 3
    assert len(SORT_AT) == LISTED // TOP and PARTS * POOL_TILES % ROWS == 0
    assert len(JOIN) == TILES and JOIN[0] == 0 and TILES % POOL_TILES == 0 and POOL_TILES % LISTS == 0

    def tiles(q):
        here = [t for t in range(TILES) if JOIN[t] <= q < JOIN[t] + NB]
        return here[0], len(here)

    def after_block(q):
        return sum(tiles(x)[1] for x in range(q + 1))

    most_tiles = max(tiles(q)[1] for q in range(BLOCKS))

    def due(q):
        def step(c):
            t, j = divmod(c, PARTS)
            return max(0, JOIN[t - 1] - 2 - (j + 1) * (JOIN[t - 1] - JOIN[t]) // PARTS)
        return [c for c in range(PARTS, CHUNKS) if step(c) == q]

    assert sorted(sum(map(due, range(BLOCKS)), [])) == list(range(PARTS, CHUNKS))

    def gathered(c):
        return CH * (c // ROWS + 1)

    w_view = proj.rearrange("(k p) n -> p k n", p=P)
    out_view = out.rearrange("(m p) n -> p m n", p=P)
    ids_view = ids.rearrange("(m p) s -> p m s", p=P)
    bias_view = bias.rearrange("(b n) -> b n", n=BW)

    ctx = ExitStack()
    with ctx:
        def sb(name, shape, dt):
            return ctx.enter_context(nc.sbuf_tensor(name, shape, dt))

        def sem(name):
            return ctx.enter_context(nc.semaphore(name))

        ids_sb = sb("ids_sb", [P, TILES, SEQ], I32)
        shift = sb("shift", [P, SEQ], F32)
        key = sb("key", [P, SEQ], F32)
        top = sb("top", [P, LISTED], F32)
        index = sb("index", [P, LISTS, LISTED], U32)
        count = sb("count", [P, TILES], F32)
        count1 = sb("count1", [P, TILES], F32)
        inv_count = sb("inv_count", [P, TILES], F32)
        limit = sb("limit", [P, MORE], I32)
        over = sb("over", [P, TILES, MORE], F32)
        ones = sb("ones", [P, 1], F32)
        zero = sb("zero", [P, 1], F32)
        hit = sb("hit", [1, TILES, MORE], F32)
        rounds_f = sb("rounds_f", [1, 2 * TILES], F32)
        need = sb("need", [1, 2 * TILES], I32)
        rows = sb("rows", [P, ROWS, CH, HID], F32)
        sums = sb("sums", [P, CH, HID], F32)
        total = sb("total", [P, HID], F32)
        mean = sb("mean", [P, HID], F32)
        ident = sb("ident", [P, P], F32)
        mean_hi = sb("mean_hi", [P, TILES, K * P], F32R)
        mean_lo = sb("mean_lo", [P, TILES, K * P], F32R)
        fb_key = sb("fb_key", [P, SEQ + AGAIN], F32)
        fb_top = sb("fb_top", [P, TOP], F32)
        fb_index = sb("fb_index", [P, TOP], U32)
        fb_rows = sb("fb_rows", [P, BACK + 1, HID], F32)
        w_raw = sb("w_raw", [P, RAW, K, BW], F32)
        w_hi = sb("w_hi", [P, SPLIT, K, BW], F32R)
        w_lo = sb("w_lo", [P, SPLIT, K, BW], F32R)
        bias_raw = sb("bias_raw", [BIAS_ROWS, BW], F32)
        bias_parts = sb("bias_parts", [BIAS_ROWS, BW], BF16)
        pick = sb("pick", [BIAS_ROWS, NB], BF16)
        bias_sb = sb("bias_sb", [P, BIAS, BW], F32)
        stage = sb("stage", [P, STAGE, most_tiles, BW], F32)
        valid = stage[:, 0].rearrange("p m n -> p (m n)")[:, 0:TILES * SEQ].rearrange("p (t s) -> p t s", t=TILES)

        acc = ctx.enter_context(nc.psum_tensor("acc", [P, BANKS, 512], F32))
        turned = ctx.enter_context(nc.psum_tensor("turned", [P, K * P], F32))
        overs = turned[0:1]
        spread = ctx.enter_context(nc.psum_tensor("spread", [P, 512], F32))

        s_ids0 = sem("first_ids_loaded")
        s_ids = sem("ids_loaded")
        s_const = sem("constants_set")
        s_ident = sem("identity_built")
        s_sort = sem("sort_steps")
        s_index = sem("index_ready")
        s_count = sem("count_steps")
        s_overs = sem("overs_summed")
        s_need = sem("needs_ready")
        s_zeroed = sem("chunks_zeroed")
        s_rows = [sem(f"rows_gathered{i}") for i in range(ROWS)]
        s_summed = sem("chunks_summed")
        s_folded = sem("sums_folded")
        s_mean = sem("means_ready")
        s_turned = sem("means_turned")
        s_mean_hi = sem("mean_hi_ready")
        s_mean_lo = sem("mean_lo_ready")
        s_fb = [sem(f"branch_steps{t}") for t in range(TILES)]
        s_fb_go = sem("branch_index_ready")
        s_fb_rows = sem("branch_rows_gathered")
        s_pool_passed = sem("pool_passed")
        s_dve_passed = sem("dve_passed")
        s_raw = [sem(f"w_loaded{i}") for i in range(RAW)]
        s_bias_zero = sem("bias_rows_zeroed")
        s_bias_raw = sem("bias_loaded")
        s_bias_hi = sem("bias_high_ready")
        s_bias_parts = sem("bias_split_steps")
        s_pick = sem("pick_steps")
        s_spread = sem("bias_spread")
        s_bias = sem("bias_ready")
        s_w_hi = sem("w_hi_ready")
        s_w_lo = sem("w_lo_ready")
        s_product = sem("products_done")
        s_moved = sem("banks_freed")
        s_stored = [sem(f"stored{i}") for i in range(STAGE)]

        block = ctx.enter_context(nc.Block())

        def further(engine, t):
            return (engine.value_load(need[0:1, bass.ds(t + TILES, 1)], min_val=0, max_val=MORE),
                    engine.value_load(need[0:1, bass.ds(t, 1)], min_val=0, max_val=MORE * TILES))

        @block.sync
        def _(sp):
            def load_w(q):
                if q >= RAW:
                    sp.wait_ge(s_w_lo, q - RAW + 1)
                sp.dma_start(w_raw[:, q % RAW], w_view[:, :, bass.ts(q % NB, BW)]).then_inc(s_raw[q % RAW], 16)

            sp.dma_start(ids_sb[:, 0], ids_view[:, 0]).then_inc(s_ids0, 16)
            sp.dma_start(ids_sb[:, 1:], ids_view[:, 1:]).then_inc(s_ids, 16)
            sp.wait_ge(s_bias_zero, 1)
            for at in PART_AT:
                sp.dma_start(bias_raw[at:at + NB], bias_view).then_inc(s_bias_raw, 16)
            for q in range(LEAD_W):
                load_w(q)
            for q in range(BLOCKS):
                if q + LEAD_W < BLOCKS:
                    load_w(q + LEAD_W)
                first, n = tiles(q)
                sp.wait_ge(s_moved, BANKS + after_block(q))
                sp.dma_start(out_view[:, first:first + n, bass.ts(q % NB, BW)],
                             stage[:, q % STAGE, 0:n]).then_inc(s_stored[q % STAGE], 16)
            for i in range(STAGE):
                sp.wait_ge(s_stored[i], 16 * len(range(i, BLOCKS, STAGE)))

        @block.gpsimd
        def _(pool):
            def alone():
                pool.sem_inc(s_pool_passed, 1)

            pool.memset(ident[:], 0.0).then_inc(s_ident, 1)
            pool.wait_ge(s_ident, 1)
            pool.affine_select(out=ident[:], in_=ident[:], compare_op=ALU.not_equal, fill=1.0, base=0,
                               pattern=[[-1, P]], channel_multiplier=1).then_inc(s_ident, 1)

            pool.iota(limit[:], pattern=[[TOP, MORE]], base=FAST, channel_multiplier=0).then_inc(s_ident, 1)

            def gather(dst, column):
                return pool.indirect_dma_start(
                    out=dst, out_offset=None, in_=table,
                    in_offset=bass.IndirectOffsetOnAxis(ap=column, axis=0),
                    bounds_check=ITEMS - 1, oob_is_err=False)

            with pool.Fori(0, TILES // POOL_TILES) as i:
                for tt in range(POOL_TILES):
                    t = POOL_TILES * i + tt
                    for j in range(PARTS):
                        buf = (PARTS * tt + j) % ROWS
                        if CH * j % TOP == 0:
                            pool.wait_ge(s_index, LISTED // TOP * t + (CH * j // TOP + 1))
                        pool.wait_ge(s_zeroed, PARTS * t + (j + 1))
                        alone()
                        for c in range(CH):
                            gather(rows[:, buf, c, :], index[:, tt % LISTS, CH * j + c:CH * j + c + 1]).then_inc(
                                s_rows[buf], 16)
                    pool.wait_ge(s_need, 1)
                    rounds, rounds_before = further(pool, t)
                    with pool.If(rounds > 0):
                        with pool.Fori(0, rounds) as r:
                            for turn in range(TURNS):
                                pool.wait_ge(s_fb_go, TURNS * (rounds_before + r) + (turn + 1))
                                alone()
                                for c in range(BACK):
                                    gather(fb_rows[:, c, :], fb_index[:, BACK * turn + c:BACK * turn + c + 1]).then_inc(
                                        s_fb_rows, 16)

        @block.scalar
        def _(act):
            def clear(c):
                if c >= ROWS:
                    act.wait_ge(s_summed, c - ROWS + 1)
                nc.scalar.activation(rows[:, c % ROWS].rearrange("p c d -> p (c d)"),
                                     zero[:, 0:1].to_broadcast([P, CH * HID]), ACT.Copy).then_inc(s_zeroed, 1)

            def w_high(q):
                if q >= SPLIT:
                    act.wait_ge(s_product, after_block(q - SPLIT))
                act.wait_ge(s_raw[q % RAW], 16 * (q // RAW + 1))
                nc.scalar.activation(w_hi[:, q % SPLIT], w_raw[:, q % RAW], ACT.Copy).then_inc(s_w_hi, 1)

            def mean_high(t):
                act.wait_ge(s_turned, t + 1)
                nc.scalar.activation(mean_hi[:, t], turned[:], ACT.Copy).then_inc(s_mean_hi, 1)

            def bias_copy(q):
                act.wait_ge(s_spread, q + 1)
                if q >= BIAS:
                    act.wait_ge(s_moved, BANKS + after_block(q - BIAS))
                nc.scalar.activation(bias_sb[:, q % BIAS], spread[:, 0:BW], ACT.Copy).then_inc(s_bias, 1)

            act.wait_ge(s_const, 1)
            for c in range(ROWS):
                clear(c)
            act.wait_ge(s_bias_raw, 16 * len(PART_AT))
            nc.scalar.activation(bias_parts[:], bias_raw[:], ACT.Copy).then_inc(s_bias_hi, 1)
            for q in range(RAW):
                w_high(q)
            for c in range(PARTS):
                clear(c + ROWS)
                if c in BIAS_AFTER:
                    bias_copy(BIAS_AFTER.index(c))
                if c in HIGH_AFTER:
                    w_high(RAW + HIGH_AFTER.index(c))
            mean_high(0)
            for q in range(BLOCKS):
                if q + LEAD_BIAS < BLOCKS:
                    bias_copy(q + LEAD_BIAS)
                for c in due(q):
                    if c + ROWS < CHUNKS:
                        clear(c + ROWS)
                if q + SPLIT < BLOCKS:
                    w_high(q + SPLIT)
                if q + 2 in JOIN:
                    mean_high(JOIN.index(q + 2))

        @block.vector
        def _(dve):
            def alone():
                dve.sem_inc(s_dve_passed, 1)

            def keys(dst, t, step, at):
                dve.tensor_scalar(shift[:], ids_sb[:, t], 0.0, float(ITEMS), ALU.is_lt, ALU.mult).then_inc(step, 1)
                dve.wait_ge(step, at + 1)
                dve.tensor_tensor(dst, shift[:], ids_sb[:, t], ALU.add).then_inc(step, 1)
                dve.wait_ge(step, at + 2)
                dve.tensor_scalar(dst, dst, 0.0, -1.0, ALU.max, ALU.mult).then_inc(step, 1)
                dve.wait_ge(step, at + 3)
                dve.tensor_scalar(dst, dst, float(ITEMS), 0.0, ALU.add, ALU.max).then_inc(step, 1)
                dve.wait_ge(step, at + 4)

            def sort(t, rounds=range(LISTED // TOP)):
                at = SORT_OPS * t
                if 0 in rounds:
                    keys(key[:], t, s_sort, at)
                for r in rounds:
                    eight = top[:, TOP * r:TOP * (r + 1)]
                    dve.max(eight, key[:]).then_inc(s_sort, 1)
                    dve.wait_ge(s_sort, at + KEY_OPS + 2 * r + 1)
                    dve.tensor_scalar(index[:, t % LISTS, TOP * r:TOP * (r + 1)], eight, -1.0, float(ITEMS),
                                      ALU.mult, ALU.add).then_inc(s_index, 1)
                    dve.match_replace(key[:], eight, key[:], -1.0).then_inc(s_sort, 1)
                    dve.wait_ge(s_sort, at + KEY_OPS + 2 * r + 2)

            def add_further(t):
                rounds, rounds_before = further(dve, t)
                with dve.If(rounds > 0):
                    keys(fb_key[:, 0:SEQ], t, s_fb[t], 0)
                    at = KEY_OPS
                    for r in range(LISTED // TOP):
                        dve.max(fb_top[:], fb_key[:, 0:SEQ]).then_inc(s_fb[t], 1)
                        dve.wait_ge(s_fb[t], at + 2 * r + 1)
                        dve.match_replace(fb_key[:, 0:SEQ], fb_top[:], fb_key[:, 0:SEQ], -1.0).then_inc(s_fb[t], 1)
                        dve.wait_ge(s_fb[t], at + 2 * r + 2)
                    at += 2 * (LISTED // TOP) + 1
                    dve.tensor_copy(fb_key[:, SEQ:], fb_top[:, TOP - AGAIN:]).then_inc(s_fb[t], 1)
                    dve.wait_ge(s_fb[t], at)
                    per_round = 2 * TURNS + 2
                    with dve.Fori(0, rounds) as r:
                        step = per_round * r + at
                        dve.max(fb_top[:], fb_key[:]).then_inc(s_fb[t], 1)
                        dve.wait_ge(s_fb[t], step + 1)
                        alone()
                        dve.match_replace(fb_key[:], fb_top[:], fb_key[:], -1.0).then_inc(s_fb[t], 1)
                        dve.tensor_scalar(fb_index[:], fb_top[:], -1.0, float(ITEMS), ALU.mult, ALU.add)
                        for turn in range(TURNS):
                            dve.memset(fb_rows[:, 0:BACK, :], 0.0).then_inc(s_fb_go, 1)
                            done = TURNS * (rounds_before + r) + (turn + 1)
                            dve.wait_ge(s_fb_rows, 16 * BACK * done)
                            dve.tensor_reduce(fb_rows[:, BACK, :],
                                              fb_rows[:, 0:BACK, :].rearrange("p c d -> p d c"),
                                              AX.X, ALU.add).then_inc(s_fb[t], 1)
                            dve.wait_ge(s_fb[t], step + (2 + 2 * turn + 1))
                            dve.tensor_tensor(sums[:, 0, :], sums[:, 0, :], fb_rows[:, BACK, :], ALU.add).then_inc(
                                s_fb[t], 1)
                            dve.wait_ge(s_fb[t], step + (2 + 2 * turn + 2))
                            alone()

            def add_chunk(c):
                t, j = divmod(c, PARTS)
                if j == 0:
                    return
                if j == 1:
                    dve.wait_ge(s_rows[(c - 1) % ROWS], 16 * gathered(c - 1))
                else:
                    dve.wait_ge(s_summed, c)
                if j == PARTS - 1:
                    add_further(t)
                dve.wait_ge(s_rows[c % ROWS], 16 * gathered(c))
                dve.tensor_tensor(sums[:], rows[:, (c - 1) % ROWS] if j == 1 else sums[:], rows[:, c % ROWS],
                                  ALU.add).then_inc(s_summed, 2 if j == 1 else 1)
                if j == PARTS - 1:
                    half = CH // 2
                    dve.wait_ge(s_summed, c + 1)
                    dve.tensor_tensor(sums[:, 0:half], sums[:, 0:half], sums[:, half:], ALU.add).then_inc(s_folded, 1)
                    dve.wait_ge(s_folded, 2 * t + 1)
                    dve.tensor_tensor(total[:], sums[:, 0], sums[:, 1], ALU.add).then_inc(s_folded, 1)

            def mean_of(t):
                dve.wait_ge(s_folded, 2 * (t + 1))
                dve.tensor_scalar(mean[:], total[:], inv_count[:, t:t + 1], None, ALU.mult).then_inc(s_mean, 1)

            def mean_low(t):
                dve.wait_ge(s_mean_hi, t + 1)
                dve.tensor_tensor(mean_lo[:, t], turned[:], mean_hi[:, t].bitcast(F32), ALU.subtract).then_inc(
                    s_mean_lo, 1)

            def w_low(q):
                dve.wait_ge(s_w_hi, q + 1)
                dve.tensor_tensor(w_lo[:, q % SPLIT], w_raw[:, q % RAW], w_hi[:, q % SPLIT].bitcast(F32),
                                  ALU.subtract).then_inc(s_w_lo, 1)

            def move_out(q):
                first, n = tiles(q)
                dve.wait_ge(s_bias, q + 1)
                if q >= STAGE:
                    dve.wait_ge(s_stored[q % STAGE], 16 * (q // STAGE))
                for r in range(after_block(q) - n, after_block(q)):
                    m = r - (after_block(q) - n)
                    dve.wait_ge(s_product, r + 1)
                    dve.tensor_tensor(stage[:, q % STAGE, m], acc[:, r % BANKS, 0:BW],
                                      bias_sb[:, q % BIAS], ALU.add).then_inc(s_moved, 1)

            dve.memset(zero[:], 0.0).then_inc(s_const, 1)
            dve.memset(bias_raw[:], 0.0).then_inc(s_bias_zero, 1)
            dve.memset(ones[:], 1.0).then_inc(s_moved, BANKS)
            dve.wait_ge(s_ids0, 16)
            sort(0)
            dve.wait_ge(s_ids, 16)
            dve.tensor_scalar(valid, ids_sb[:], float(ITEMS), None, ALU.is_lt).then_inc(s_count, 1)
            dve.wait_ge(s_count, 1)
            dve.tensor_reduce(count[:], valid, AX.X, ALU.add).then_inc(s_count, 1)
            dve.wait_ge(s_count, 2)
            dve.wait_ge(s_ident, 3)
            dve.tensor_tensor(over[:], count[:].rearrange("p (t o) -> p t o", o=1).to_broadcast([P, TILES, MORE]),
                              limit[:].rearrange("p (o r) -> p o r", o=1).to_broadcast([P, TILES, MORE]),
                              ALU.is_gt).then_inc(s_count, 1)
            dve.tensor_scalar(count1[:], count[:], 1.0, None, ALU.max).then_inc(s_count, 1)
            dve.wait_ge(s_count, 4)
            dve.reciprocal(inv_count[:], count1[:]).then_inc(s_count, 1)
            dve.wait_ge(s_ident, 2)
            low, lowest = (slice(at, at + NB) for at in PART_AT[1:])
            dve.tensor_tensor(pick[:], ident[0:BIAS_ROWS, 0:NB], ident[0:BIAS_ROWS, low], ALU.add).then_inc(s_pick, 1)
            dve.wait_ge(s_pick, 1)
            dve.tensor_tensor(pick[:], pick[:], ident[0:BIAS_ROWS, lowest], ALU.add).then_inc(s_pick, 1)
            dve.wait_ge(s_bias_hi, 1)
            dve.tensor_tensor(bias_parts[low], bias_raw[low], bias_parts[low], ALU.subtract)
            dve.tensor_tensor(bias_raw[lowest], bias_raw[lowest], bias_parts[lowest], ALU.subtract).then_inc(s_bias_parts, 1)
            dve.wait_ge(s_bias_parts, 1)
            dve.tensor_copy(bias_parts[lowest], bias_raw[lowest]).then_inc(s_bias_parts, 1)
            dve.wait_ge(s_bias_parts, 2)
            dve.tensor_tensor(bias_parts[lowest], bias_raw[lowest], bias_parts[lowest], ALU.subtract).then_inc(
                s_bias_parts, 1)
            for c in range(PARTS):
                add_chunk(c)
                if c == 2:
                    sort(1)
                if c == 3:
                    dve.wait_ge(s_count, 5)
                    dve.wait_ge(s_overs, 1)
                    dve.tensor_scalar(hit[:].rearrange("o t r -> o (t r)"), overs[0:1, 0:TILES * MORE], 1.0, None,
                                      ALU.min).then_inc(s_count, 1)
                    dve.wait_ge(s_count, 6)
                    dve.memset(rounds_f[:, 0:1], 0.0)
                    for t in range(1, TILES):
                        dve.tensor_reduce(rounds_f[:, t:t + 1], hit[:, 0:t].rearrange("o t r -> o (t r)"), AX.X, ALU.add)
                    dve.tensor_reduce(rounds_f[:, TILES:], hit[:], AX.X, ALU.add).then_inc(s_count, 1)
                    dve.wait_ge(s_count, 7)
                    dve.tensor_copy(need[:], rounds_f[:]).then_inc(s_need, 1)
                    dve.wait_ge(s_need, 1)
                if c in LOW_AFTER:
                    w_low(LOW_AFTER.index(c))
            mean_of(0)
            mean_low(0)
            for q in range(len(LOW_AFTER), LEAD_LOW):
                w_low(q)
            for q in range(BLOCKS):
                for c in due(q):
                    add_chunk(c)
                    if c // PARTS + 1 < TILES:
                        sort(c // PARTS + 1, [r for r in range(LISTED // TOP) if c % PARTS == SORT_AT[r]])
                if q + 2 in JOIN:
                    mean_of(JOIN.index(q + 2))
                if q + LEAD_LOW < BLOCKS:
                    w_low(q + LEAD_LOW)
                move_out(q)
                if q + 2 in JOIN:
                    mean_low(JOIN.index(q + 2))

        @block.tensor
        def _(pe):
            def turn(t):
                pe.wait_ge(s_mean, t + 1)
                if t:
                    pe.wait_ge(s_mean_lo, t)
                for k in range(K):
                    last = nc.tensor.transpose(turned[:, k * P:(k + 1) * P], mean[:, k * P:(k + 1) * P], ident[:])
                last.then_inc(s_turned, 1)

            def spread_bias(q, j):
                if q:
                    pe.wait_ge(s_bias, j + q)
                block = (j + q) % NB
                nc.tensor.matmul(spread[:, 0:BW], pick[:, bass.ds(block, 1)].to_broadcast([BIAS_ROWS, P]), bias_parts[:],
                                 start=True, stop=True).then_inc(s_spread, 1)

            def products(q, j):
                first, n = tiles(q)
                if q + LEAD_BIAS < BLOCKS:
                    spread_bias(q + LEAD_BIAS, j)
                pe.wait_ge(s_w_lo, j + (q + 1))
                buf = (j + q) % SPLIT
                for m in range(n):
                    r = j * n + (after_block(q) - n + m)
                    pe.wait_ge(s_moved, r + 1)
                    bank = acc[:, bass.ds(r % BANKS, 1), 0:BW].rearrange("p o n -> p (o n)")
                    for k in range(K):
                        hi, lo = (x[:, first + m, k * P:(k + 1) * P] for x in (mean_hi, mean_lo))
                        high, low = (x[:, bass.ds(buf, 1), k].rearrange("p o n -> p (o n)") for x in (w_hi, w_lo))
                        nc.tensor.matmul(bank, hi, high, start=k == 0, stop=False)
                        nc.tensor.matmul(bank, hi, low, start=False, stop=False)
                        last = nc.tensor.matmul(bank, lo, high, start=False, stop=k == K - 1)
                    last.then_inc(s_product, 1)

            pe.wait_ge(s_count, 3)
            pe.wait_ge(s_moved, BANKS)
            nc.tensor.matmul(overs[0:1, 0:TILES * MORE], ones[:], over[:].rearrange("p t r -> p (t r)"),
                             start=True, stop=True).then_inc(s_overs, 1)
            pe.wait_ge(s_pick, 2)
            pe.wait_ge(s_bias_parts, 3)
            for q in range(LEAD_BIAS):
                spread_bias(q, 0)
            pe.wait_ge(s_ident, 2)
            turn(0)
            q = 0
            while q < BLOCKS:
                first, n = tiles(q)
                pe.wait_ge(s_mean_lo, first + n)
                if q + 1 in JOIN:
                    turn(JOIN.index(q + 1))
                run = 1
                while q + run < BLOCKS and tiles(q + run) == (first, n) and q + run + 1 not in JOIN \
                        and q + run != BLOCKS - LEAD_BIAS:
                    run += 1
                if run > 1:
                    with pe.Fori(0, run) as j:
                        products(q, j)
                else:
                    products(q, 0)
                q += run


_INS = ["r_sequence_ids", "L0_rec_emb_table", "L0_rec_proj_w", "L0_rec_proj_b"]


def kernel(**inputs):
    import numpy as _np
    import concourse.bacc as _bacc
    from concourse import mybir as _mybir
    from concourse.bass_utils import run_bass_kernel_spmd as _run

    nc = _bacc.Bacc("TRN2", target_bir_lowering=False, num_devices=1)
    arrays, args = {}, []
    for name in _INS:
        a = _np.ascontiguousarray(inputs[name])
        arrays[f"in_{name}_dram"] = a
        args.append(nc.dram_tensor(f"in_{name}_dram", a.shape, _mybir.dt.from_np(a.dtype), kind="ExternalInput").ap())
    shape = (arrays["in_r_sequence_ids_dram"].shape[0], arrays["in_L0_rec_proj_w_dram"].shape[1])
    args.append(nc.dram_tensor("out_0_dram", shape, _mybir.dt.float32, kind="ExternalOutput").ap())
    mean_embedding_projection(nc, *args)
    r = _run(nc, [arrays], core_ids=[0])
    return r.results[0]["out_0_dram"]
```
